# Optimizing a Trainium2 kernel written in Bass

```python
import numpy as np
import jax
import jax.numpy as jnp

def _softmax(x, axis=-1):
    return jax.nn.softmax(x, axis=axis)

def _gelu(x):
    return jax.nn.gelu(x, approximate=True)

def _silu(x):
    return jax.nn.silu(x)

def _sigmoid(x):
    return jax.nn.sigmoid(x)

def _layernorm(x, axis=-1, eps=1e-05):
    m = jnp.mean(x, axis=axis, keepdims=True)
    v = jnp.var(x, axis=axis, keepdims=True)
    return (x - m) / jnp.sqrt(v + eps)

def _scatter_add(tgt, idx, src, axis=0):
    return tgt.at[idx].add(src)

def _segment_sum(src, seg, n):
    return jax.ops.segment_sum(src, seg, n)
kernel_name = 'mk_adaln_ffn_d1_seqx_r2_20b41e'

def setup_inputs(seed: int=0):
    np.random.seed(seed)
    _w = jnp.asarray

    def _rec_inputs():
        import jax
        import jax.numpy as jnp
        _rk = jax.random.key(seed)
        x = -0.000125 + 0.9999 * jax.random.normal(jax.random.fold_in(_rk, 1), (128, 128, 1024), jnp.float32)
        _lenS = 128 - jax.random.randint(jax.random.fold_in(_rk, 7), (128,), 0, max(1, 128 // 4) + 1, jnp.int32)
        _lenS2 = 128 - jax.random.randint(jax.random.fold_in(_rk, 8), (128,), 0, max(1, 128 // 4) + 1, jnp.int32)
        itok_B_0_7 = jax.random.randint(jax.random.fold_in(_rk, 11), (128,), 0, 8, jnp.int32)
        fside_8xS_0 = -0.00162727 + 0.0609077 * jax.random.normal(jax.random.fold_in(_rk, 12), (8, 128), jnp.float32)
        return (x, itok_B_0_7, fside_8xS_0)
    x, itok_B_0_7, fside_8xS_0 = _rec_inputs()

    def _L0_cond_setup():
        import jax, jax.numpy as jnp
        import numpy as np
        B, C, T = (64, 128, 1024)
        D, N = (128, 8)
        key = jax.random.key(seed)
        k_x, k_s, k_w, k_b = jax.random.split(key, 4)
        scale = 1.0 / np.sqrt(C)
        x = jax.random.normal(k_x, (B, C, T), dtype=jnp.float32)
        subjects = jax.random.randint(k_s, (B,), 0, N, dtype=jnp.int64)
        weights = jax.random.normal(k_w, (N, C, D), dtype=jnp.float32) * scale
        bias = jax.random.normal(k_b, (N, D), dtype=jnp.float32) * scale
        return {'x': x, 'subjects': subjects, 'weights': weights, 'bias': bias}
    _L0_cond_all = _L0_cond_setup()
    _L0_cond_in = {k: v for k, v in _L0_cond_all.items() if k in ('weights',)}
    del _L0_cond_all

    def _L0_ffn_setup():
        import jax, jax.numpy as jnp
        import numpy as np
        D_IN = 1024
        D_OUT = 1024
        EPS = 1e-05
        key = jax.random.key(seed)
        k_x, k_w = jax.random.split(key)
        x = jax.random.normal(k_x, (8, 1024, D_IN), dtype=jnp.float32)
        weight = jax.random.normal(k_w, (D_OUT, D_IN), dtype=jnp.float32)
        gamma = jnp.ones((D_OUT,), dtype=jnp.float32)
        beta = jnp.zeros((D_OUT,), dtype=jnp.float32)
        ln_weight = jnp.ones((D_IN,), dtype=jnp.float32)
        ln_bias = jnp.zeros((D_IN,), dtype=jnp.float32)
        return {'x': x, 'weight': weight, 'gamma': gamma, 'beta': beta, 'ln_weight': ln_weight, 'ln_bias': ln_bias}
    _L0_ffn_all = _L0_ffn_setup()
    _L0_ffn_in = {k: v for k, v in _L0_ffn_all.items() if k in ('weight', 'gamma', 'beta', 'ln_weight', 'ln_bias')}
    del _L0_ffn_all
    return {'x': x, 'itok_B_0_7': itok_B_0_7, 'fside_8xS_0': fside_8xS_0, 'L0_cond_weights': _L0_cond_in['weights'], 'L0_ffn_weight': _L0_ffn_in['weight'], 'L0_ffn_gamma': _L0_ffn_in['gamma'], 'L0_ffn_beta': _L0_ffn_in['beta'], 'L0_ffn_ln_weight': _L0_ffn_in['ln_weight'], 'L0_ffn_ln_bias': _L0_ffn_in['ln_bias']}

def reference(x, itok_B_0_7, fside_8xS_0, L0_cond_weights, L0_ffn_weight, L0_ffn_gamma, L0_ffn_beta, L0_ffn_ln_weight, L0_ffn_ln_bias):
    import jax
    import jax.numpy as jnp

    def _L0_cond_ref(x, subjects, weights, bias):
        import jax, jax.numpy as jnp
        import numpy as np
        B, C, T = (64, 128, 1024)
        D, N = (128, 8)
        w = weights[subjects]
        b = bias[subjects]
        out = jnp.einsum('bct,bcd->bdt', x, w)
        out = out + b[:, :, None]
        return out

    def _L0_ffn_ref(x, weight, gamma, beta, ln_weight, ln_bias):
        import jax, jax.numpy as jnp
        import numpy as np
        D_IN = 1024
        D_OUT = 1024
        EPS = 1e-05
        mean = jnp.mean(x, axis=-1, keepdims=True)
        var = jnp.mean(jnp.square(x - mean), axis=-1, keepdims=True)
        xn = (x - mean) * jax.lax.rsqrt(var + EPS) * ln_weight + ln_bias
        quant_w = jnp.sign(weight)
        scale = jnp.max(jnp.abs(weight))
        out = jnp.einsum('bsk,ok->bso', xn, quant_w)
        return out * scale * gamma + beta
    x = x + _L0_ffn_ref(_L0_cond_ref(x, itok_B_0_7, L0_cond_weights, fside_8xS_0), L0_ffn_weight, L0_ffn_gamma, L0_ffn_beta, L0_ffn_ln_weight, L0_ffn_ln_bias)
    return x

_drawn_inputs = setup_inputs


def setup_inputs(seed=0):
    import zlib

    import numpy as np

    out = dict(_drawn_inputs(seed))
    spreads = {'L0_ffn_gamma': (1.0, 0.2),
     'L0_ffn_beta': (0.0, 0.1),
     'L0_ffn_ln_weight': (1.0, 0.2),
     'L0_ffn_ln_bias': (0.0, 0.1)}
    factors = {}
    for name, (base, spread) in spreads.items():
        noise = np.random.default_rng([zlib.crc32(name.encode()), seed]).standard_normal(out[name].shape)
        drawn = base * np.exp(spread * noise) if base else spread * noise
        out[name] = jnp.asarray(drawn.astype(out[name].dtype))
    for name, factor in factors.items():
        out[name] = (out[name] * factor).astype(out[name].dtype)
    return out
```

```python
from contextlib import ExitStack

import numpy as np

import concourse.bass as bass
from concourse import mybir

B, C, T = 128, 128, 1024
S = 8
P = 128
K = T // P
HALF = 512
EPS = 1e-5
UNROLL = 4


def adaln_ffn(nc, x, subject, bias, cond_w, weight, gamma, beta, ln_w, ln_b, out):
    f32, f32r, bf16 = mybir.dt.float32, mybir.dt.float32r, mybir.dt.bfloat16
    ACT, ALU, AX = mybir.ActivationFunctionType, mybir.AluOpType, mybir.AxisListType

    ctx = ExitStack()
    with ctx:
        def sb(name, shape, dt=f32):
            return ctx.enter_context(nc.sbuf_tensor(name, shape, dt))

        def ps(name, shape, dt=f32):
            return ctx.enter_context(nc.psum_tensor(name, shape, dt))

        def sem(name):
            return ctx.enter_context(nc.semaphore(name))

        signT = sb("signT", [P, K, T], f32r)
        subj_w = sb("subj_w", [P, S, C])
        bias_dev = sb("bias_dev", [P, S, C])
        out_gain = sb("out_gain", [P, T])
        out_shift = sb("out_shift", [P, T])
        lnw_t = sb("lnw_t", [P, K])
        lnb_t = sb("lnb_t", [P, K])
        subj_id = sb("subj_id", [1, B], mybir.dt.int32)
        ones = sb("ones", [P, 1])
        ident = sb("ident", [P, P], bf16)
        w_max = sb("w_max", [P, K])
        w_max_row = sb("w_max_row", [P, 1])
        w_max_all = sb("w_max_all", [P, 1])
        w_rows = sb("w_rows", [P, K, T])
        w_sign = sb("w_sign", [P, K, T], bf16)
        xs = sb("xs", [P, UNROLL, T])
        xc = sb("xc", [P, 2, T])
        x_copy = sb("x_copy", [P, T])
        x_sum = sb("x_sum", [P, 2])
        x_mean_neg = sb("x_mean_neg", [P, 2])
        h = sb("h", [P, 2, T])
        hw = sb("hw", [P, 2, T])
        hi = sb("hi", [P, 2, T], f32r)
        lo = sb("lo", [P, 2, T], f32r)
        sq = sb("sq", [P, T])
        sq_part = sb("sq_part", [P, 2, C])
        var_eps = sb("var_eps", [P, 2])
        rstd = sb("rstd", [P, 2])
        neg_half = sb("neg_half", [P, 1])
        scaled = sb("scaled", [P, T])
        ys = sb("ys", [P, 2, T])

        big_ps = ps("big_ps", [P, 2, T])
        h_ps = ps("h_ps", [P, T])
        var_ps = ps("var_ps", [P, HALF])
        turn_ps = [big_ps[:, n // 2, (n % 2) * HALF:(n % 2 + 1) * HALF].bitcast(bf16)
                   .rearrange("p (k o) -> p k o", k=K) for n in range(4)]

        x_loaded = [sem(f"x_loaded{n}") for n in range(UNROLL)]
        y_stored = [sem(f"y_stored{n}") for n in range(2)]
        w_loaded = [sem(f"w_loaded{n}") for n in range(K)]
        subj_w_loaded = sem("subj_w_loaded")
        bias_loaded = sem("bias_loaded")
        lnw_loaded = sem("lnw_loaded")
        lnb_loaded = sem("lnb_loaded")
        subj_id_loaded = sem("subj_id_loaded")
        gamma_loaded = sem("gamma_loaded")
        beta_loaded = sem("beta_loaded")
        const_made = sem("const_made")
        ones_made = sem("ones_made")
        signed = sem("signed")
        turned = sem("turned")
        kept_act = sem("kept_act")
        kept_dve = sem("kept_dve")
        w_max_step = sem("w_max_step")
        w_max_done = sem("w_max_done")
        bias_step = sem("bias_step")
        gain_done = sem("gain_done")
        shift_step = sem("shift_step")
        summed = sem("summed")
        mean_done = sem("mean_done")
        centred = sem("centred")
        projected = sem("projected")
        h_done = sem("h_done")
        squared = sem("squared")
        hw_done = sem("hw_done")
        hi_done = sem("hi_done")
        lo_done = sem("lo_done")
        sq_part_done = sem("sq_part_done")
        var_done = sem("var_done")
        var_eps_done = sem("var_eps_done")
        rstd_done = sem("rstd_done")
        big_done = sem("big_done")
        big_read = sem("big_read")
        shifted = sem("shifted")
        y_done = sem("y_done")

        block = ctx.enter_context(nc.Block())

        @block.sync
        def _(sp):
            def load(b, slot):
                sp.dma_start(xs[:, slot, :], x[bass.ds(b, 1), :, :].rearrange("b c t -> c (b t)"))\
                  .then_inc(x_loaded[slot], 16)

            def store(b, buf):
                sp.wait_ge(y_done, b + 1)
                sp.dma_start(out[bass.ds(b, 1), :, :].rearrange("b c t -> c (b t)"), ys[:, buf, :])\
                  .then_inc(y_stored[buf], 16)

            load(0, 0)
            sp.dma_start(subj_w[:], cond_w.rearrange("s c d -> c s d")).then_inc(subj_w_loaded, 16)
            for j in range(K):
                sp.dma_start(w_rows[:, j, :], weight[j * P:(j + 1) * P, :]).then_inc(w_loaded[j], 16)
                if j == 1:
                    load(1, 1)
            for b in range(2, UNROLL):
                load(b, b)
            with sp.Fori(0, B // UNROLL - 1) as g:
                for u in range(UNROLL):
                    store(UNROLL * g + u, u % 2)
                    load(UNROLL * g + (u + UNROLL), u)
            for b in range(B - UNROLL, B):
                store(b, b % 2)
            for buf in range(2):
                sp.wait_ge(y_stored[buf], 16 * (B // 2))

        @block.scalar
        def _(act):
            def flat(v):
                return v.rearrange("(a n) -> a n", a=1)

            act.dma_start(lnw_t[:], ln_w.rearrange("(k p) -> p k", p=P), allow_slow_non_contiguous=True)\
               .then_inc(lnw_loaded, 16)
            act.dma_start(lnb_t[:], ln_b.rearrange("(k p) -> p k", p=P), allow_slow_non_contiguous=True)\
               .then_inc(lnb_loaded, 16)
            act.dma_start(subj_id[:], flat(subject)).then_inc(subj_id_loaded, 16)
            act.dma_start(bias_dev[:], bias.rearrange("s d -> (s d)").partition_broadcast(P)
                          .rearrange("p (s d) -> p s d", s=S)).then_inc(bias_loaded, 16)
            act.dma_start(out_gain[:], gamma.partition_broadcast(P)).then_inc(gamma_loaded, 16)
            act.dma_start(out_shift[:], beta.partition_broadcast(P)).then_inc(beta_loaded, 16)

            def centre(b, u, loads, steady):
                par = u % 2
                act.wait_ge(x_loaded[u % UNROLL], 16 * loads)
                nc.scalar.activation(x_copy[:], xs[:, u % UNROLL, :], ACT.Copy,
                                     accum_out=x_sum[:, par:par + 1]).then_inc(summed, 1)
                act.wait_ge(summed, b + 1)
                nc.scalar.activation(x_mean_neg[:, par:par + 1], x_sum[:, par:par + 1], ACT.Copy,
                                     scale=-1.0 / T).then_inc(mean_done, 1)
                act.wait_ge(mean_done, b + 1)
                if steady:
                    act.wait_ge(projected, b - 1)
                nc.scalar.activation(xc[:, par, :], xs[:, u % UNROLL, :], ACT.Identity,
                                     bias=x_mean_neg[:, par:par + 1]).then_inc(centred, 1)

            def high_part(b, par, steady):
                if steady:
                    act.wait_ge(big_done, b)
                nc.scalar.activation(hi[:, par, :], hw[:, par, :], ACT.Copy).then_inc(hi_done, 1)

            def square_and_scale(b, par, steady, first=False):
                act.wait_ge(h_done, b + 1)
                if not first:
                    act.wait_ge(sq_part_done, b)
                nc.scalar.activation(sq[:], h[:, par, :], ACT.Square).then_inc(squared, 1)
                if steady:
                    act.wait_ge(lo_done, b)
                for k in range(K):
                    last = nc.scalar.activation(hw[:, par, k * P:(k + 1) * P],
                                                h[:, par, k * P:(k + 1) * P],
                                                ACT.Copy, scale=lnw_t[:, k:k + 1])
                last.then_inc(hw_done, 1)
                act.wait_ge(hw_done, b + 2)
                high_part(b, par, steady)

            def keep(j):
                act.wait_ge(turned, j + 1)
                nc.scalar.activation(signT[:, :, j * P:(j + 1) * P], turn_ps[j % 4], ACT.Copy)\
                  .then_inc(kept_act, 1)

            centre(0, 0, 1, False)
            for j in range(K):
                act.wait_ge(w_loaded[j], 16)
                nc.scalar.activation(w_sign[:, j, :], w_rows[:, j, :], ACT.Sign).then_inc(signed, 1)
                if j == 2:
                    act.wait_ge(hw_done, 1)
                    high_part(-1, 1, False)
                    act.wait_ge(lnw_loaded, 16)
                    square_and_scale(0, 0, False, first=True)
                if j == 4:
                    centre(1, 1, 1, False)
                if j % 2 == 1:
                    keep(j - 1)

            def window(i, u, loads, steady):
                centre(i + 2, u + 2, loads + (u + 2) // UNROLL, steady or i + 2 >= 2)
                square_and_scale(i + 1, (u + 1) % 2, steady or i + 1 >= 1)

            for i in range(UNROLL):
                window(i, i, 1, False)
            with act.Fori(1, B // UNROLL - 1) as g:
                for u in range(UNROLL):
                    window(UNROLL * g + u, u, g + 1, True)
            for u in range(UNROLL):
                i = B - UNROLL + u
                if i + 2 < B:
                    centre(i + 2, u + 2, B // UNROLL, True)
                if i + 1 < B:
                    square_and_scale(i + 1, (u + 1) % 2, True)

        @block.tensor
        def _(pe):
            def project(b, par, first=False):
                s = pe.value_load(subj_id[0:1, bass.ds(b, 1)], min_val=0, max_val=S - 1)
                pe.wait_ge(centred, b + 1)
                if not first:
                    pe.wait_ge(h_done, b)
                for k in range(K):
                    last = nc.tensor.matmul(h_ps[:, k * P:(k + 1) * P], xc[:, par, k * P:(k + 1) * P],
                                            subj_w[:, bass.ds(s, 1), :].rearrange("c a d -> c (a d)"),
                                            start=True, stop=True)
                last.then_inc(projected, 1)

            def sum_squares(b, par, first=False):
                pe.wait_ge(sq_part_done, b + 1)
                if not first:
                    pe.wait_ge(var_eps_done, b)
                nc.tensor.matmul(var_ps[:, par:par + 1], sq_part[:, par, :], ones[:, :],
                                 start=True, stop=True).then_inc(var_done, 1)

            def large_product(b, par, steady):
                pe.wait_ge(hi_done, b + 2)
                pe.wait_ge(lo_done, b + 2)
                if steady:
                    pe.wait_ge(big_read, b)
                for k in range(K):
                    for n, part in enumerate((hi, lo)):
                        for o in (0, HALF):
                            last = nc.tensor.matmul(big_ps[:, par, o:o + HALF],
                                                    part[:, par, k * P:(k + 1) * P],
                                                    signT[:, k, o:o + HALF],
                                                    start=(k == 0 and n == 0),
                                                    stop=(k == K - 1 and n == 1))
                last.then_inc(big_done, 1)

            pe.wait_ge(subj_id_loaded, 16)
            pe.wait_ge(subj_w_loaded, 16)
            project(0, 0, first=True)
            pe.wait_ge(const_made, 3)
            for j in range(K):
                pe.wait_ge(signed, j + 1)
                if j >= 4:
                    if j % 2:
                        pe.wait_ge(kept_dve, (j - 4) // 2 + 1)
                    else:
                        pe.wait_ge(kept_act, (j - 4) // 2 + 1)
                for k in range(K):
                    last = nc.tensor.transpose(turn_ps[j % 4][:, k, :], w_sign[:, j, k * P:(k + 1) * P],
                                               ident[:])
                last.then_inc(turned, 1)
            pe.wait_ge(kept_act, K // 2)
            pe.wait_ge(kept_dve, K // 2)
            large_product(-1, 1, False)
            pe.wait_ge(ones_made, 1)

            def window(i, u, steady):
                project(i + 1, (u + 1) % 2)
                sum_squares(i, u % 2, first=not steady and i == 0)
                large_product(i, u % 2, steady or i >= 1)

            for i in range(UNROLL):
                window(i, i, False)
            with pe.Fori(1, B // UNROLL - 1) as g:
                for u in range(UNROLL):
                    window(UNROLL * g + u, u, True)
            for u in range(UNROLL):
                i = B - UNROLL + u
                if i + 1 < B:
                    project(i + 1, (u + 1) % 2)
                sum_squares(i, u % 2)
                large_product(i, u % 2, True)

        @block.vector
        def _(dve):
            def output(b, u, steady):
                par = u % 2
                dve.wait_ge(big_done, b + 2)
                dve.wait_ge(rstd_done, b + 1)
                nc.vector.scalar_tensor_tensor(scaled[:], big_ps[:, par, :], rstd[:, par:par + 1],
                                               out_gain[:], ALU.mult, ALU.mult).then_inc(big_read, 1)
                dve.wait_ge(big_read, b + 2)
                dve.wait_ge(shifted, b + 1)
                return par

            def add_and_hand_over(u, stores):
                if stores is not None:
                    dve.wait_ge(y_stored[u % 2], 16 * stores)
                nc.vector.tensor_tensor(ys[:, u % 2, :], scaled[:], xs[:, u % UNROLL, :], ALU.add)\
                  .then_inc(y_done, 1)

            def take_h(b, u, steady):
                par = u % 2
                s = dve.value_load(subj_id[0:1, bass.ds(b, 1)], min_val=0, max_val=S - 1)
                dve.wait_ge(projected, b + 1)
                if steady:
                    dve.wait_ge(squared, b - 1)
                    dve.wait_ge(hw_done, b)
                nc.vector.tensor_tensor(h[:, par, :].rearrange("p (k d) -> p k d", k=K),
                                        h_ps[:].rearrange("p (k d) -> p k d", k=K),
                                        bias_dev[:, bass.ds(s, 1), :].broadcast_to([P, K, C]),
                                        ALU.add).then_inc(h_done, 1)

            def shift_x(b, u):
                dve.wait_ge(centred, b + 1)
                nc.vector.tensor_tensor(xs[:, u % UNROLL, :], xs[:, u % UNROLL, :], out_shift[:],
                                        ALU.add).then_inc(shifted, 1)

            def low_part(b, par, steady):
                dve.wait_ge(hi_done, b + 2)
                if steady:
                    dve.wait_ge(big_done, b)
                nc.vector.tensor_tensor(lo[:, par, :], hw[:, par, :], hi[:, par, :].bitcast(f32),
                                        ALU.subtract).then_inc(lo_done, 1)

            def sum_chunks(b, par, steady):
                dve.wait_ge(squared, b + 1)
                if steady:
                    dve.wait_ge(var_done, b - 1)
                nc.vector.tensor_reduce(sq_part[:, par, :], sq[:].rearrange("p (k d) -> p d k", k=K),
                                        AX.X, ALU.add).then_inc(sq_part_done, 1)

            def variance(b, par, steady):
                dve.wait_ge(var_done, b + 1)
                if steady:
                    dve.wait_ge(rstd_done, b - 1)
                nc.vector.tensor_scalar(var_eps[:, par:par + 1], var_ps[:, par:par + 1], 1.0 / T, EPS,
                                        ALU.mult, ALU.add).then_inc(var_eps_done, 1)

            def keep(j):
                dve.wait_ge(turned, j + 1)
                nc.vector.tensor_copy(signT[:, :, j * P:(j + 1) * P], turn_ps[j % 4])\
                  .then_inc(kept_dve, 1)

            nc.vector.memset(ones[:], 1.0).then_inc(ones_made, 1)
            dve.wait_ge(lnb_loaded, 16)
            nc.vector.tensor_copy(hw[:, 1, :].rearrange("p (k d) -> p k d", k=K),
                                  lnb_t[:].rearrange("p (k a) -> p k a", a=1)
                                  .broadcast_to([P, K, P])).then_inc(hw_done, 1)
            dve.wait_ge(bias_loaded, 16)
            nc.vector.tensor_scalar(h[:, 1, :], bias_dev[:].rearrange("p s d -> p (s d)"), float(T),
                                    1.0 / T, ALU.mult, ALU.mult).then_inc(bias_step, 1)
            dve.wait_ge(bias_step, 1)
            nc.vector.tensor_tensor(bias_dev[:].rearrange("p s d -> p (s d)"),
                                    bias_dev[:].rearrange("p s d -> p (s d)"), h[:, 1, :],
                                    ALU.subtract).then_inc(bias_step, 1)
            dve.wait_ge(bias_step, 2)
            dve.wait_ge(subj_id_loaded, 16)
            for j in range(K):
                dve.wait_ge(w_loaded[j], 16)
                nc.vector.tensor_reduce(w_max[:, j:j + 1], w_rows[:, j, :], AX.X, ALU.max,
                                        apply_absolute_value=True).then_inc(w_max_step, 1)
                if j == 1:
                    take_h(0, 0, False)
                if j == 3:
                    low_part(-1, 1, False)
                    low_part(0, 0, False)
                    sum_chunks(0, 0, False)
                if j >= 2 and j % 2 == 0:
                    keep(j - 1)
            dve.wait_ge(w_max_step, K)
            nc.vector.tensor_reduce(w_max_row[:], w_max[:], AX.X, ALU.max).then_inc(w_max_step, 1)
            keep(K - 1)
            dve.wait_ge(gamma_loaded, 16)
            dve.wait_ge(w_max_done, 1)
            nc.vector.tensor_scalar(out_gain[:], out_gain[:], w_max_all[:, 0:1], None, ALU.mult)\
              .then_inc(gain_done, 1)
            dve.wait_ge(gain_done, 1)
            dve.wait_ge(big_done, 1)
            nc.vector.tensor_tensor(scaled[:], big_ps[:, 1, :], out_gain[:], ALU.mult)\
              .then_inc(big_read, 1)
            dve.wait_ge(big_read, 1)
            dve.wait_ge(beta_loaded, 16)
            nc.vector.tensor_tensor(out_shift[:], scaled[:], out_shift[:], ALU.add)\
              .then_inc(shift_step, 1)
            dve.wait_ge(shift_step, 1)
            shift_x(0, 0)
            shift_x(1, 1)

            def window(i, u, stores, steady):
                if steady or i >= 1:
                    output(i - 1, u - 1, True)
                    add_and_hand_over(u - 1, stores)
                take_h(i + 1, u + 1, steady or i + 1 >= 2)
                variance(i, u % 2, steady or i >= 2)
                shift_x(i + 2, u + 2)
                sum_chunks(i + 1, (u + 1) % 2, steady or i + 1 >= 2)
                low_part(i + 1, (u + 1) % 2, True)

            for i in range(UNROLL):
                window(i, i, (i - 1) // 2 if i >= 3 else None, False)
            with dve.Fori(1, B // UNROLL - 1) as g:
                for u in range(UNROLL):
                    window(UNROLL * g + u, u, (UNROLL // 2) * g + (u - 1) // 2, True)
            for u in range(UNROLL):
                i = B - UNROLL + u
                output(i - 1, u - 1, True)
                add_and_hand_over(u - 1, (i - 1) // 2)
                if i + 1 < B:
                    take_h(i + 1, u + 1, True)
                variance(i, u % 2, True)
                if i + 2 < B:
                    shift_x(i + 2, u + 2)
                if i + 1 < B:
                    sum_chunks(i + 1, (u + 1) % 2, True)
                    low_part(i + 1, (u + 1) % 2, True)
            output(B - 1, UNROLL - 1, True)
            add_and_hand_over(UNROLL - 1, (B - 1) // 2)

        @block.gpsimd
        def _(pool):
            nc.gpsimd.memset(neg_half[:], -0.5).then_inc(const_made, 1)
            nc.gpsimd.memset(ident[:], 0.0).then_inc(const_made, 1)
            pool.wait_ge(const_made, 2)
            nc.gpsimd.affine_select(out=ident[:], in_=ident[:], compare_op=ALU.not_equal, fill=1.0,
                                    base=0, pattern=[[-1, P]], channel_multiplier=1)\
              .then_inc(const_made, 1)
            pool.wait_ge(w_max_step, K + 1)
            nc.gpsimd.partition_all_reduce(w_max_all[:], w_max_row[:], P, bass.bass_isa.ReduceOp.max)\
              .then_inc(w_max_done, 1)

            def inverse_deviation(b, par, steady):
                pool.wait_ge(var_eps_done, b + 1)
                if steady:
                    pool.wait_ge(big_read, b)
                nc.gpsimd.tensor_tensor(rstd[:, par:par + 1], var_eps[:, par:par + 1], neg_half[:],
                                        ALU.pow).then_inc(rstd_done, 1)

            for b in range(2):
                inverse_deviation(b, b, False)
            with pool.Fori(1, B // 2) as g:
                for par in range(2):
                    inverse_deviation(2 * g + par, par, True)


_INS = ["x", "itok_B_0_7", "fside_8xS_0", "L0_cond_weights", "L0_ffn_weight", "L0_ffn_gamma",
        "L0_ffn_beta", "L0_ffn_ln_weight", "L0_ffn_ln_bias"]


def kernel(**inputs):
    import concourse.bacc as bacc
    from concourse.bass_utils import run_bass_kernel_spmd

    nc = bacc.Bacc("TRN2", target_bir_lowering=False, num_devices=1)
    arrays, aps = {}, []
    for name in _INS:
        a = np.ascontiguousarray(inputs[name])
        arrays[f"in_{name}"] = a
        aps.append(nc.dram_tensor(f"in_{name}", a.shape, mybir.dt.from_np(a.dtype),
                                  kind="ExternalInput").ap())
    aps.append(nc.dram_tensor("out_0", (B, C, T), mybir.dt.float32, kind="ExternalOutput").ap())
    adaln_ffn(nc, *aps)
    result = run_bass_kernel_spmd(nc, [arrays], core_ids=[0])
    return result.results[0]["out_0"]
```

```python
from contextlib import ExitStack

import numpy as np

import concourse.bass as bass
from concourse import mybir

B, C, T = 128, 128, 1024
S = 8
P = 128
K = T // P
HALF = 512
EPS = 1e-5
UNROLL = 4


def adaln_ffn(nc, x, subject, bias, cond_w, weight, gamma, beta, ln_w, ln_b, out):
    f32, f32r, bf16 = mybir.dt.float32, mybir.dt.float32r, mybir.dt.bfloat16
    ACT, ALU, AX = mybir.ActivationFunctionType, mybir.AluOpType, mybir.AxisListType

    ctx = ExitStack()
    with ctx:
        def sb(name, shape, dt=f32):
            return ctx.enter_context(nc.sbuf_tensor(name, shape, dt))

        def ps(name, shape, dt=f32):
            return ctx.enter_context(nc.psum_tensor(name, shape, dt))

        def sem(name):
            return ctx.enter_context(nc.semaphore(name))

        signT = sb("signT", [P, K, T], f32r)
        subj_w = sb("subj_w", [P, S, C])
        bias_dev = sb("bias_dev", [P, S, C])
        out_gain = sb("out_gain", [P, T])
        out_shift = sb("out_shift", [P, T])
        lnw_t = sb("lnw_t", [P, K])
        lnb_t = sb("lnb_t", [P, K])
        subj_id = sb("subj_id", [1, B], mybir.dt.int32)
        ones = sb("ones", [P, 1])
        ident = sb("ident", [P, P], bf16)
        w_max = sb("w_max", [P, K])
        w_max_row = sb("w_max_row", [P, 1])
        w_max_all = sb("w_max_all", [P, 1])
        w_rows = sb("w_rows", [P, K, T])
        w_sign = sb("w_sign", [P, K, T], bf16)
        xs = sb("xs", [P, UNROLL, T])
        xc = sb("xc", [P, 2, T])
        x_copy = sb("x_copy", [P, T])
        x_sum = sb("x_sum", [P, 2])
        x_mean_neg = sb("x_mean_neg", [P, 2])
        h = sb("h", [P, 2, T])
        hw = sb("hw", [P, 2, T])
        hi = sb("hi", [P, 2, T], f32r)
        lo = sb("lo", [P, 2, T], f32r)
        sq = sb("sq", [P, T])
        sq_part = sb("sq_part", [P, 2, C])
        var_eps = sb("var_eps", [P, 2])
        rstd = sb("rstd", [P, 2])
        neg_half = sb("neg_half", [P, 1])
        scaled = sb("scaled", [P, T])
        ys = sb("ys", [P, 2, T])

        big_ps = ps("big_ps", [P, 2, T])
        h_ps = ps("h_ps", [P, T])
        var_ps = ps("var_ps", [P, HALF])
        turn_ps = [big_ps[:, n // 2, (n % 2) * HALF:(n % 2 + 1) * HALF].bitcast(bf16)
                   .rearrange("p (k o) -> p k o", k=K) for n in range(4)]

        x_loaded = [sem(f"x_loaded{n}") for n in range(UNROLL)]
        y_stored = [sem(f"y_stored{n}") for n in range(2)]
        w_loaded = [sem(f"w_loaded{n}") for n in range(K)]
        subj_w_loaded = sem("subj_w_loaded")
        bias_loaded = sem("bias_loaded")
        lnw_loaded = sem("lnw_loaded")
        lnb_loaded = sem("lnb_loaded")
        subj_id_loaded = sem("subj_id_loaded")
        gamma_loaded = sem("gamma_loaded")
        beta_loaded = sem("beta_loaded")
        const_made = sem("const_made")
        ones_made = sem("ones_made")
        signed = sem("signed")
        turned = sem("turned")
        kept = sem("kept")
        w_max_step = sem("w_max_step")
        w_max_done = sem("w_max_done")
        bias_step = sem("bias_step")
        gain_done = sem("gain_done")
        shift_step = sem("shift_step")
        summed = sem("summed")
        mean_done = sem("mean_done")
        centred = sem("centred")
        projected = sem("projected")
        h_done = sem("h_done")
        squared = sem("squared")
        hw_done = sem("hw_done")
        hi_done = sem("hi_done")
        lo_done = sem("lo_done")
        sq_part_done = sem("sq_part_done")
        var_done = sem("var_done")
        var_eps_done = sem("var_eps_done")
        rstd_done = sem("rstd_done")
        big_done = sem("big_done")
        big_read = sem("big_read")
        shifted = sem("shifted")
        y_done = sem("y_done")
        last_half_done = sem("last_half_done")
        last_half_scaled = sem("last_half_scaled")
        last_half_y_done = sem("last_half_y_done")

        block = ctx.enter_context(nc.Block())

        @block.sync
        def _(sp):
            def load(b, slot):
                sp.dma_start(xs[:, slot, :], x[bass.ds(b, 1), :, :].rearrange("b c t -> c (b t)"))\
                  .then_inc(x_loaded[slot], 16)

            def store(b, buf):
                sp.wait_ge(y_done, b + 1)
                sp.dma_start(out[bass.ds(b, 1), :, :].rearrange("b c t -> c (b t)"), ys[:, buf, :])\
                  .then_inc(y_stored[buf], 16)

            for j in range(K):
                sp.dma_start(w_rows[:, j, :], weight[j * P:(j + 1) * P, :]).then_inc(w_loaded[j], 16)
            load(0, 0)
            sp.dma_start(subj_w[:], cond_w.rearrange("s c d -> c s d")).then_inc(subj_w_loaded, 16)
            sp.dma_start(bias_dev[:], bias.rearrange("s d -> (s d)").partition_broadcast(P)
                         .rearrange("p (s d) -> p s d", s=S)).then_inc(bias_loaded, 16)
            load(1, 1)
            sp.dma_start(out_gain[:], gamma.partition_broadcast(P)).then_inc(gamma_loaded, 16)
            sp.dma_start(out_shift[:], beta.partition_broadcast(P)).then_inc(beta_loaded, 16)
            for b in range(2, UNROLL):
                load(b, b)
            with sp.Fori(0, B // UNROLL - 1) as g:
                for u in range(UNROLL):
                    store(UNROLL * g + u, u % 2)
                    load(UNROLL * g + (u + UNROLL), u)
            for b in range(B - UNROLL, B - 1):
                store(b, b % 2)
            for n, o in enumerate((0, HALF)):
                sp.wait_ge(last_half_y_done, n + 1)
                sp.dma_start(out[B - 1, :, o:o + HALF], ys[:, 1, o:o + HALF]).then_inc(y_stored[1], 16)
            sp.wait_ge(y_stored[0], 16 * (B // 2))
            sp.wait_ge(y_stored[1], 16 * (B // 2 + 1))

        @block.scalar
        def _(act):
            act.dma_start(lnb_t[:], ln_b.rearrange("(k p) -> p k", p=P), allow_slow_non_contiguous=True)\
               .then_inc(lnb_loaded, 16)
            act.dma_start(subj_id[:], subject.rearrange("(a n) -> a n", a=1)).then_inc(subj_id_loaded, 16)
            act.dma_start(lnw_t[:], ln_w.rearrange("(k p) -> p k", p=P), allow_slow_non_contiguous=True)\
               .then_inc(lnw_loaded, 16)

            def centre(b, u, loads, steady):
                par = u % 2
                act.wait_ge(x_loaded[u % UNROLL], 16 * loads)
                nc.scalar.activation(x_copy[:], xs[:, u % UNROLL, :], ACT.Copy,
                                     accum_out=x_sum[:, par:par + 1]).then_inc(summed, 1)
                act.wait_ge(summed, b + 1)
                nc.scalar.activation(x_mean_neg[:, par:par + 1], x_sum[:, par:par + 1], ACT.Copy,
                                     scale=-1.0 / T).then_inc(mean_done, 1)
                act.wait_ge(mean_done, b + 1)
                if steady:
                    act.wait_ge(projected, b - 1)
                nc.scalar.activation(xc[:, par, :], xs[:, u % UNROLL, :], ACT.Identity,
                                     bias=x_mean_neg[:, par:par + 1]).then_inc(centred, 1)

            def high_part(b, par, steady):
                if steady:
                    act.wait_ge(big_done, b)
                nc.scalar.activation(hi[:, par, :], hw[:, par, :], ACT.Copy).then_inc(hi_done, 1)

            def scale_and_square(b, par, steady, first=False):
                act.wait_ge(h_done, b + 1)
                if steady:
                    act.wait_ge(lo_done, b)
                for k in range(K):
                    last = nc.scalar.activation(hw[:, par, k * P:(k + 1) * P],
                                                h[:, par, k * P:(k + 1) * P],
                                                ACT.Copy, scale=lnw_t[:, k:k + 1])
                last.then_inc(hw_done, 1)
                act.wait_ge(hw_done, b + 2)
                high_part(b, par, steady)
                if not first:
                    act.wait_ge(sq_part_done, b)
                nc.scalar.activation(sq[:], h[:, par, :], ACT.Square).then_inc(squared, 1)

            for j in range(K):
                act.wait_ge(w_loaded[j], 16)
                nc.scalar.activation(w_sign[:, j, :], w_rows[:, j, :], ACT.Sign).then_inc(signed, 1)
                if j == 2:
                    act.wait_ge(hw_done, 1)
                    high_part(-1, 1, False)
            centre(0, 0, 1, False)
            centre(1, 1, 1, False)
            act.wait_ge(lnw_loaded, 16)
            scale_and_square(0, 0, False, first=True)

            def window(i, u, loads, steady):
                centre(i + 2, u + 2, loads + (u + 2) // UNROLL, steady or i + 2 >= 2)
                scale_and_square(i + 1, (u + 1) % 2, steady or i + 1 >= 1)

            for i in range(UNROLL):
                window(i, i, 1, False)
            with act.Fori(1, B // UNROLL - 1) as g:
                for u in range(UNROLL):
                    window(UNROLL * g + u, u, g + 1, True)
            for u in range(UNROLL):
                i = B - UNROLL + u
                if i + 2 < B:
                    centre(i + 2, u + 2, B // UNROLL, True)
                if i + 1 < B:
                    scale_and_square(i + 1, (u + 1) % 2, True)

        @block.tensor
        def _(pe):
            def project(b, par, first=False):
                s = pe.value_load(subj_id[0:1, bass.ds(b, 1)], min_val=0, max_val=S - 1)
                pe.wait_ge(centred, b + 1)
                if not first:
                    pe.wait_ge(h_done, b)
                for k in range(K):
                    last = nc.tensor.matmul(h_ps[:, k * P:(k + 1) * P], xc[:, par, k * P:(k + 1) * P],
                                            subj_w[:, bass.ds(s, 1), :].rearrange("c a d -> c (a d)"),
                                            start=True, stop=True)
                last.then_inc(projected, 1)

            def sum_squares(b, par, first=False):
                pe.wait_ge(sq_part_done, b + 1)
                if not first:
                    pe.wait_ge(var_eps_done, b)
                nc.tensor.matmul(var_ps[:, par:par + 1], sq_part[:, par, :], ones[:, :],
                                 start=True, stop=True).then_inc(var_done, 1)

            def large_product(b, par, steady, with_projection_of_0=False):
                pe.wait_ge(hi_done, b + 2)
                pe.wait_ge(lo_done, b + 2)
                if steady:
                    pe.wait_ge(big_read, b)
                for k in range(K):
                    for part in (hi, lo):
                        for o in (0, HALF):
                            last = product_step(par, k, part, o)
                    if k == 0 and with_projection_of_0:
                        project(0, 0, first=True)
                last.then_inc(big_done, 1)

            def product_step(par, k, part, o):
                return nc.tensor.matmul(big_ps[:, par, o:o + HALF], part[:, par, k * P:(k + 1) * P],
                                        signT[:, k, o:o + HALF], start=(k == 0 and part is hi),
                                        stop=(k == K - 1 and part is lo))

            def last_large_product(b, par):
                pe.wait_ge(hi_done, b + 2)
                pe.wait_ge(lo_done, b + 2)
                pe.wait_ge(big_read, b)
                for o in (0, HALF):
                    for k in range(K):
                        for part in (hi, lo):
                            last = product_step(par, k, part, o)
                    last.then_inc(last_half_done, 1)

            pe.wait_ge(const_made, 3)
            for j in range(K):
                pe.wait_ge(signed, j + 1)
                if j >= 4:
                    pe.wait_ge(kept, j - 3)
                for k in range(K):
                    last = nc.tensor.transpose(turn_ps[j % 4][:, k, :], w_sign[:, j, k * P:(k + 1) * P],
                                               ident[:])
                last.then_inc(turned, 1)
            pe.wait_ge(kept, K)
            pe.wait_ge(subj_id_loaded, 16)
            pe.wait_ge(subj_w_loaded, 16)
            large_product(-1, 1, False, with_projection_of_0=True)
            pe.wait_ge(ones_made, 1)

            def window(i, u, steady):
                project(i + 1, (u + 1) % 2)
                sum_squares(i, u % 2, first=not steady and i == 0)
                large_product(i, u % 2, steady or i >= 1)

            for i in range(UNROLL):
                window(i, i, False)
            with pe.Fori(1, B // UNROLL - 1) as g:
                for u in range(UNROLL):
                    window(UNROLL * g + u, u, True)
            for u in range(UNROLL):
                i = B - UNROLL + u
                if i + 1 < B:
                    project(i + 1, (u + 1) % 2)
                sum_squares(i, u % 2)
                if i + 1 < B:
                    large_product(i, u % 2, True)
                else:
                    last_large_product(i, u % 2)

        @block.vector
        def _(dve):
            def scale_product(b, u):
                par = u % 2
                dve.wait_ge(big_done, b + 2)
                dve.wait_ge(rstd_done, b + 1)
                nc.vector.scalar_tensor_tensor(scaled[:], big_ps[:, par, :], rstd[:, par:par + 1],
                                               out_gain[:], ALU.mult, ALU.mult).then_inc(big_read, 1)

            def add_x(b, u, stores):
                dve.wait_ge(big_read, b + 2)
                dve.wait_ge(shifted, b + 1)
                if stores is not None:
                    dve.wait_ge(y_stored[u % 2], 16 * stores)
                nc.vector.tensor_tensor(ys[:, u % 2, :], scaled[:], xs[:, u % UNROLL, :], ALU.add)\
                  .then_inc(y_done, 1)

            def take_h(b, u, steady):
                par = u % 2
                s = dve.value_load(subj_id[0:1, bass.ds(b, 1)], min_val=0, max_val=S - 1)
                dve.wait_ge(projected, b + 1)
                if steady:
                    dve.wait_ge(squared, b - 1)
                    dve.wait_ge(hw_done, b)
                nc.vector.tensor_tensor(h[:, par, :].rearrange("p (k d) -> p k d", k=K),
                                        h_ps[:].rearrange("p (k d) -> p k d", k=K),
                                        bias_dev[:, bass.ds(s, 1), :].broadcast_to([P, K, C]),
                                        ALU.add).then_inc(h_done, 1)

            def shift_x(b, u):
                dve.wait_ge(centred, b + 1)
                nc.vector.tensor_tensor(xs[:, u % UNROLL, :], xs[:, u % UNROLL, :], out_shift[:],
                                        ALU.add).then_inc(shifted, 1)

            def low_part(b, par, steady):
                dve.wait_ge(hi_done, b + 2)
                if steady:
                    dve.wait_ge(big_done, b)
                nc.vector.tensor_tensor(lo[:, par, :], hw[:, par, :], hi[:, par, :].bitcast(f32),
                                        ALU.subtract).then_inc(lo_done, 1)

            def sum_chunks(b, par, steady):
                dve.wait_ge(squared, b + 1)
                if steady:
                    dve.wait_ge(var_done, b - 1)
                nc.vector.tensor_reduce(sq_part[:, par, :], sq[:].rearrange("p (k d) -> p d k", k=K),
                                        AX.X, ALU.add).then_inc(sq_part_done, 1)

            def variance(b, par, steady):
                dve.wait_ge(var_done, b + 1)
                if steady:
                    dve.wait_ge(rstd_done, b - 1)
                nc.vector.tensor_scalar(var_eps[:, par:par + 1], var_ps[:, par:par + 1], 1.0 / T, EPS,
                                        ALU.mult, ALU.add).then_inc(var_eps_done, 1)

            def keep(j):
                dve.wait_ge(turned, j + 1)
                nc.vector.tensor_copy(signT[:, :, j * P:(j + 1) * P], turn_ps[j % 4])\
                  .then_inc(kept, 1)

            nc.vector.memset(ones[:], 1.0).then_inc(ones_made, 1)
            dve.wait_ge(lnb_loaded, 16)
            nc.vector.tensor_copy(hw[:, 1, :].rearrange("p (k d) -> p k d", k=K),
                                  lnb_t[:].rearrange("p (k a) -> p k a", a=1)
                                  .broadcast_to([P, K, P])).then_inc(hw_done, 1)

            def block_max(j):
                dve.wait_ge(w_loaded[j], 16)
                nc.vector.tensor_reduce(w_max[:, j:j + 1], w_rows[:, j, :], AX.X, ALU.max,
                                        apply_absolute_value=True).then_inc(w_max_step, 1)

            block_max(0)
            block_max(1)
            for j in range(K):
                keep(j)
                if j == 3:
                    low_part(-1, 1, False)
            dve.wait_ge(bias_loaded, 16)
            nc.vector.tensor_scalar(h[:, 1, :], bias_dev[:].rearrange("p s d -> p (s d)"), float(T),
                                    1.0 / T, ALU.mult, ALU.mult).then_inc(bias_step, 1)
            dve.wait_ge(bias_step, 1)
            nc.vector.tensor_tensor(bias_dev[:].rearrange("p s d -> p (s d)"),
                                    bias_dev[:].rearrange("p s d -> p (s d)"), h[:, 1, :],
                                    ALU.subtract).then_inc(bias_step, 1)
            dve.wait_ge(bias_step, 2)
            dve.wait_ge(subj_id_loaded, 16)
            block_max(2)
            block_max(3)
            take_h(0, 0, False)
            for j in range(4, 7):
                block_max(j)
            low_part(0, 0, False)
            sum_chunks(0, 0, False)
            block_max(7)
            take_h(1, 1, False)
            dve.wait_ge(w_max_step, K)
            nc.vector.tensor_reduce(w_max_row[:], w_max[:], AX.X, ALU.max).then_inc(w_max_step, 1)
            dve.wait_ge(gamma_loaded, 16)
            dve.wait_ge(w_max_done, 1)
            nc.vector.tensor_scalar(out_gain[:], out_gain[:], w_max_all[:, 0:1], None, ALU.mult)\
              .then_inc(gain_done, 1)
            dve.wait_ge(gain_done, 1)
            dve.wait_ge(big_done, 1)
            nc.vector.tensor_tensor(scaled[:], big_ps[:, 1, :], out_gain[:], ALU.mult)\
              .then_inc(big_read, 1)
            dve.wait_ge(big_read, 1)
            dve.wait_ge(beta_loaded, 16)
            nc.vector.tensor_tensor(out_shift[:], scaled[:], out_shift[:], ALU.add)\
              .then_inc(shift_step, 1)
            variance(0, 0, False)
            low_part(1, 1, True)
            sum_chunks(1, 1, False)
            dve.wait_ge(shift_step, 1)

            def window(i, u, stores, steady):
                scale_product(i - 1, u - 1)
                take_h(i + 1, u + 1, True)
                if not steady and i == 1:
                    shift_x(0, 0)
                    shift_x(1, 1)
                add_x(i - 1, u - 1, stores)
                variance(i, u % 2, steady or i >= 2)
                shift_x(i + 1, u + 1)
                low_part(i + 1, (u + 1) % 2, True)
                sum_chunks(i + 1, (u + 1) % 2, True)

            for i in range(1, UNROLL):
                window(i, i, (i - 1) // 2 if i >= 3 else None, False)
            with dve.Fori(1, B // UNROLL - 1) as g:
                for u in range(UNROLL):
                    window(UNROLL * g + u, u, (UNROLL // 2) * g + (u - 1) // 2, True)
            for u in range(UNROLL):
                i = B - UNROLL + u
                scale_product(i - 1, u - 1)
                if i + 1 < B:
                    take_h(i + 1, u + 1, True)
                add_x(i - 1, u - 1, (i - 1) // 2)
                variance(i, u % 2, True)
                if i + 1 < B:
                    shift_x(i + 1, u + 1)
                    low_part(i + 1, (u + 1) % 2, True)
                    sum_chunks(i + 1, (u + 1) % 2, True)
            dve.wait_ge(rstd_done, B)
            dve.wait_ge(shifted, B)
            dve.wait_ge(y_stored[1], 16 * (B // 2 - 1))
            for n, o in enumerate((0, HALF)):
                cols = slice(o, o + HALF)
                dve.wait_ge(last_half_done, n + 1)
                nc.vector.scalar_tensor_tensor(scaled[:, cols], big_ps[:, 1, cols], rstd[:, 1:2],
                                               out_gain[:, cols], ALU.mult, ALU.mult)\
                  .then_inc(last_half_scaled, 1)
                dve.wait_ge(last_half_scaled, n + 1)
                nc.vector.tensor_tensor(ys[:, 1, cols], scaled[:, cols], xs[:, UNROLL - 1, cols],
                                        ALU.add).then_inc(last_half_y_done, 1)

        @block.gpsimd
        def _(pool):
            nc.gpsimd.memset(neg_half[:], -0.5).then_inc(const_made, 1)
            nc.gpsimd.memset(ident[:], 0.0).then_inc(const_made, 1)
            pool.wait_ge(const_made, 2)
            nc.gpsimd.affine_select(out=ident[:], in_=ident[:], compare_op=ALU.not_equal, fill=1.0,
                                    base=0, pattern=[[-1, P]], channel_multiplier=1)\
              .then_inc(const_made, 1)
            pool.wait_ge(w_max_step, K + 1)
            nc.gpsimd.partition_all_reduce(w_max_all[:], w_max_row[:], P, bass.bass_isa.ReduceOp.max)\
              .then_inc(w_max_done, 1)

            def inverse_deviation(b, par, steady):
                pool.wait_ge(var_eps_done, b + 1)
                if steady:
                    pool.wait_ge(big_read, b)
                nc.gpsimd.tensor_tensor(rstd[:, par:par + 1], var_eps[:, par:par + 1], neg_half[:],
                                        ALU.pow).then_inc(rstd_done, 1)

            for b in range(2):
                inverse_deviation(b, b, False)
            with pool.Fori(1, B // 2) as g:
                for par in range(2):
                    inverse_deviation(2 * g + par, par, True)


_INS = ["x", "itok_B_0_7", "fside_8xS_0", "L0_cond_weights", "L0_ffn_weight", "L0_ffn_gamma",
        "L0_ffn_beta", "L0_ffn_ln_weight", "L0_ffn_ln_bias"]


def kernel(**inputs):
    import concourse.bacc as bacc
    from concourse.bass_utils import run_bass_kernel_spmd

    nc = bacc.Bacc("TRN2", target_bir_lowering=False, num_devices=1)
    arrays, aps = {}, []
    for name in _INS:
        a = np.ascontiguousarray(inputs[name])
        arrays[f"in_{name}"] = a
        aps.append(nc.dram_tensor(f"in_{name}", a.shape, mybir.dt.from_np(a.dtype),
                                  kind="ExternalInput").ap())
    aps.append(nc.dram_tensor("out_0", (B, C, T), mybir.dt.float32, kind="ExternalOutput").ap())
    adaln_ffn(nc, *aps)
    result = run_bass_kernel_spmd(nc, [arrays], core_ids=[0])
    return result.results[0]["out_0"]
```
